# Optimizing a Trainium2 kernel written in Bass

```python
import numpy as np
import jax
import jax.numpy as jnp

def _softmax(x, axis=-1):
    return jax.nn.softmax(x, axis=axis)
def _gelu(x):
    return jax.nn.gelu(x, approximate=True)
def _silu(x):
    return jax.nn.silu(x)
def _sigmoid(x):
    return jax.nn.sigmoid(x)
def _layernorm(x, axis=-1, eps=1e-5):
    m = jnp.mean(x, axis=axis, keepdims=True)
    v = jnp.var(x, axis=axis, keepdims=True)
    return (x - m) / jnp.sqrt(v + eps)
def _scatter_add(tgt, idx, src, axis=0):
    return tgt.at[idx].add(src)
def _segment_sum(src, seg, n):
    return jax.ops.segment_sum(src, seg, n)

kernel_name = 'mk_conv_preact_d1_conv_nchw128_108dbe'

def setup_inputs(seed: int = 0):
    np.random.seed(seed)
    _w = jnp.asarray
    def _rec_inputs():
        import jax
        import jax.numpy as jnp
        _gk = jax.random.key(seed)
        x = -7.109e-05 + 0.9999 * jax.random.normal(jax.random.fold_in(_gk, 1), (8, 128, 256, 256), jnp.float32)
        return x
    x = _rec_inputs()
    def _L0_conv_setup():
        import jax, jax.numpy as jnp
        import numpy as np
        EPS = 1e-06
        key = jax.random.key(seed)
        kx, kw, kb = jax.random.split(key, 3)
        C = 128
        x = jax.random.normal(kx, (8, C, 256, 256), dtype=jnp.float32)
        W = jax.random.normal(kw, (C, C), dtype=jnp.float32) * (1.0 / np.sqrt(C))
        b = jax.random.normal(kb, (C,), dtype=jnp.float32) * 0.01
        return {'x': x, 'W': W, 'b': b}
    _L0_conv_all = _L0_conv_setup()
    _L0_conv_in = {k: v for k, v in _L0_conv_all.items() if k in ('W', 'b', )}
    del _L0_conv_all

    return {
        "x": x,
        "L0_conv_W": _L0_conv_in["W"],
        "L0_conv_b": _L0_conv_in["b"],
    }

def reference(x, L0_conv_W, L0_conv_b):
    import jax
    import jax.numpy as jnp
    def _L0_conv_ref(x, W, b):
        import jax, jax.numpy as jnp
        import numpy as np
        EPS = 1e-06
        u = jnp.mean(x, axis=1, keepdims=True)
        var = jnp.var(x, axis=1, keepdims=True, ddof=1)
        s = jnp.sqrt(var)
        n_x = (x - u) / (s + EPS)
        n_x = jnp.einsum('bchw,oc->bohw', n_x, W) + b[None, :, None, None]
        return x * n_x

    def _gn(v, G=32, eps=1e-5):
        B_, C_, H_, W_ = v.shape
        g = v.reshape(B_, G, C_ // G, H_, W_)
        m = jnp.mean(g, axis=(2, 3, 4), keepdims=True)
        s = jnp.var(g, axis=(2, 3, 4), keepdims=True)
        return ((g - m) / jnp.sqrt(s + eps)).reshape(v.shape)

    def _ln_c(v, eps=1e-6):
        m = jnp.mean(v, axis=1, keepdims=True)
        s = jnp.var(v, axis=1, keepdims=True)
        return (v - m) / jnp.sqrt(s + eps)

    def _ln_t(v, eps=1e-5):
        m = jnp.mean(v, axis=-1, keepdims=True)
        s = jnp.var(v, axis=-1, keepdims=True)
        return (v - m) / jnp.sqrt(s + eps)

    def _to_tokens(v):
        B_, C_, H_, W_ = v.shape
        return v.reshape(B_, C_, H_ * W_).transpose(0, 2, 1)
    def _from_tokens(t, like):
        B_, C_, H_, W_ = like.shape
        return t.transpose(0, 2, 1).reshape(B_, C_, H_, W_)

    x = x + _L0_conv_ref(_gn(x), L0_conv_W, L0_conv_b)
    return x


_drawn_inputs = setup_inputs


def setup_inputs(seed=0):
    import zlib

    import numpy as np

    out = dict(_drawn_inputs(seed))
    spreads = {}
    factors = {'L0_conv_b': 8.0}
    for name, (base, spread) in spreads.items():
        noise = np.random.default_rng([zlib.crc32(name.encode()), seed]).standard_normal(out[name].shape)
        drawn = base * np.exp(spread * noise) if base else spread * noise
        out[name] = jnp.asarray(drawn.astype(out[name].dtype))
    for name, factor in factors.items():
        out[name] = (out[name] * factor).astype(out[name].dtype)
    return out
```

```python
import numpy as np

import concourse.bass as bass
from concourse import mybir
from contextlib import ExitStack

F32 = mybir.dt.float32
BF16 = mybir.dt.bfloat16
ALU = mybir.AluOpType
ACT = mybir.ActivationFunctionType
AXIS_X = mybir.AxisListType.X

P = 128
GROUPS = 32
GN_EPS = 1e-5
NORM_EPS = 1e-6
TINY = 1e-30

SLOT = 1024
CHUNK = 256
TILES = 4
SPLIT = 4
BANK = 512
COPIES = 32 // SPLIT

KEPT = 28
STREAM_RING = 12
STATS_RING = 4
DVE_SHARE = 4

LAG_FACTOR = 6
LAG_OUT = 7
LAG_STORE = 8
LEAD = 2

CONST_COLS = {"ident": P, "group_avg": P, "sum_rows": SPLIT * 32, "minus_bc": 1, "minus_c": 1}


def constants(channels):
    per = channels // GROUPS
    row = np.arange(P)
    piece = row % 32 // SPLIT
    parts = {
        "ident": np.eye(P),
        "group_avg": (row[:, None] // per == row[None] // per) / per,
        "sum_rows": np.tile(np.arange(32)[None] % SPLIT == np.arange(SPLIT)[:, None], (P, 1, 1)).reshape(P, -1),
        "minus_bc": -((piece == 1) | (piece == 2)).astype(np.float32)[:, None],
        "minus_c": -(piece == 2).astype(np.float32)[:, None],
    }
    const = np.concatenate([parts[k].astype(np.float32) for k in CONST_COLS], axis=1)
    pick = np.zeros((P, SPLIT, TILES), np.float32)
    for k in range(SPLIT):
        for t in range(TILES):
            pick[(row // 32 == t) & (row % SPLIT == k) & (piece < 3), k, t] = 1.0
    return const, pick.reshape(P, -1).astype(mybir.dt.np(BF16))


def norm_gate_kernel(nc, x, w, bias, const, pick, out):
    batches, _, pixels = x.shape
    slots = pixels // SLOT
    sets = slots // SPLIT
    streamed = slots - KEPT
    rounds = streamed // STREAM_RING
    stats_rounds = streamed // STATS_RING
    bn_slots = slots // DVE_SHARE
    act_slots = slots - bn_slots
    bn_pixels, act_pixels = bn_slots * SLOT, act_slots * SLOT
    assert slots * SLOT == pixels and rounds * STREAM_RING == streamed
    assert stats_rounds * STATS_RING == streamed and STATS_RING % DVE_SHARE == 0

    early = 28
    early_items = early * 3 // 2
    late_steps = slots - early - 3
    stats_step = [i * 2 // 3 if i < early_items else early + (i - early_items) * late_steps // (slots - early_items)
                  for i in range(slots)]

    def stats_items(step):
        return [i for i in range(slots) if stats_step[i] == step]

    with ExitStack() as ctx:
        def sb(name, shape, dt=F32):
            return ctx.enter_context(nc.sbuf_tensor(name, shape, dt))

        def ps(name, shape):
            return ctx.enter_context(nc.psum_tensor(name, shape, F32))

        def sem(name):
            return ctx.enter_context(nc.semaphore(name))

        kept = sb("kept", [P, KEPT, SLOT])
        stream = sb("stream", [P, STREAM_RING, SLOT])
        stats_in = sb("stats_in", [P, STATS_RING, SLOT])
        squares = sb("squares", [P, 2, SLOT])
        scaled = sb("scaled", [P, 2, SLOT])
        unused = sb("unused", [P, 2, SLOT], BF16)
        const_sb = sb("const_sb", [P, sum(CONST_COLS.values())])
        pick_sb = sb("pick_sb", [P, SPLIT * TILES], BF16)
        w_t = sb("w_t", [P, P])
        bias_sb = sb("bias_sb", [P, 1])
        w_sum = sb("w_sum", [P, 1])
        bn = sb("bn", [P, 2 * bn_slots, 6])
        act_sums = sb("act_sums", [P, 2, act_slots])
        gn = sb("gn", [P, 16])
        new_scalars = sb("new_scalars", [P, 4])
        norm_scalars = sb("norm_scalars", [P, 2])
        gate_shift = sb("gate_shift", [P, 1])
        out_shift = sb("out_shift", [P, 1])
        sum_sq = sb("sum_sq", [P, CHUNK])
        var = sb("var", [P, CHUNK])
        root = sb("root", [P, CHUNK])
        approx = sb("approx", [P, CHUNK])
        miss = sb("miss", [P, CHUNK])
        piece = sb("piece", [P, CHUNK], BF16)
        pieces = sb("pieces", [P, CHUNK], BF16)

        factor = sum_sq

        sums_ps = ps("sums_ps", [P, 2, CHUNK])
        small_ps = ps("small_ps", [P, BANK])
        factor_ps = ps("factor_ps", [P, SLOT])
        proj_ps = ps("proj_ps", [P, 2, SLOT])

        at, col = {}, 0
        for name, n in CONST_COLS.items():
            at[name] = const_sb[:, col:col + n]
            col += n
        w_in = scaled[:, 0, 0:P]
        w_centred = scaled[:, 0, P:2 * P]
        pivot = bn[:, 0, 1:2]
        neg_mean, inv_std, mean, gate_new = (new_scalars[:, i:i + 1] for i in range(4))

        consts_loaded = sem("consts_loaded")
        kept_loaded = [sem(f"kept_loaded{i}") for i in range(KEPT)]
        kept_stored = [sem(f"kept_stored{i}") for i in range(KEPT)]
        stream_loaded = [sem(f"stream_loaded{i}") for i in range(STREAM_RING)]
        stream_stored = [sem(f"stream_stored{i}") for i in range(STREAM_RING)]
        stats_loaded = [sem(f"stats_loaded{i}") for i in range(STATS_RING)]
        w_sum_ready = sem("w_sum_ready")
        w_centred_ready = sem("w_centred_ready")
        w_turned = sem("w_turned")
        w_ready = sem("w_ready")
        bn_done = sem("bn_done")
        act_done = sem("act_done")
        gn_step = sem("gn_step")
        group_mean_done = sem("group_mean_done")
        group_var_done = sem("group_var_done")
        gn_root_done = sem("gn_root_done")
        norm_scalars_set = sem("norm_scalars_set")
        gate_shift_set = sem("gate_shift_set")
        out_shift_set = sem("out_shift_set")
        normed = sem("normed")
        squared = sem("squared")
        summed = sem("summed")
        factors_spread = sem("factors_spread")
        scaled_done = sem("scaled_done")
        projected = sem("projected")
        gated = sem("gated")
        finished = sem("finished")
        sum_sq_done = sem("sum_sq_done")
        var_sum_done = sem("var_sum_done")
        var_done = sem("var_done")
        root_done = sem("root_done")
        root_sq_done = sem("root_sq_done")
        root_eps_done = sem("root_eps_done")
        approx_done = sem("approx_done")
        miss_done = sem("miss_done")
        miss_scaled = sem("miss_scaled")
        miss_squared = sem("miss_squared")
        factor_done = sem("factor_done")
        piece_a_done = sem("piece_a_done")
        rest_done = sem("rest_done")
        piece_b_done = sem("piece_b_done")
        pieces_done = sem("pieces_done")
        wait_passed = sem("wait_passed")
        GN_STEPS = 19

        def wait_apart(eng, semaphore, value):
            eng.wait_ge(semaphore, value)
            if not isinstance(value, int):
                eng.sem_inc(wait_passed, 1)

        def place(s):
            return kept[:, s, :] if s < KEPT else stream[:, (s - KEPT) % STREAM_RING, :]

        def steps(own, before, nxt):
            return range(slots if own or nxt else LAG_STORE)

        def behind(step, lag, own, before):
            s = step - lag
            return s % slots if (own if s >= 0 else before) else None

        def is_bn(i):
            return i % DVE_SHARE == 0

        def act_index(i):
            return i - i // DVE_SHARE - 1

        def wait_stats_data(eng, n, i):
            if i < streamed:
                k = i % STATS_RING
                eng.wait_ge(stats_loaded[k], (n * stats_rounds + i // STATS_RING + 1) * 16)
                return stats_in[:, k, :]
            eng.wait_ge(kept_loaded[i - streamed], (n + 1) * 16)
            return kept[:, i - streamed, :]

        def over_periods(eng, period):
            period(-1, own=False, before=False, nxt=True)
            period(0, own=True, before=False, nxt=batches > 1)
            if batches > 2:
                with eng.Fori(1, batches - 1) as b:
                    period(b, own=True, before=True, nxt=True)
            if batches > 1:
                period(batches - 1, own=True, before=True, nxt=False)
            period(batches, own=False, before=True, nxt=False)

        block = ctx.enter_context(nc.Block())

        @block.sync
        def _(sp):
            sp.dma_start(const_sb[:, :], const).then_inc(consts_loaded, 16)
            sp.dma_start(pick_sb[:, :], pick).then_inc(consts_loaded, 16)
            sp.dma_start(w_in, w).then_inc(consts_loaded, 16)
            sp.dma_start(bias_sb[:, :], bias).then_inc(consts_loaded, 16)

            def columns(s):
                return slice(s * SLOT, (s + 1) * SLOT)

            def at_batch(array, b, s):
                if isinstance(b, int):
                    return array[b, :, columns(s)]
                return array[bass.ds(b, 1), :, columns(s)].rearrange("a c n -> (a c) n")

            def load_stats(n, i, first):
                if i < streamed:
                    k = i % STATS_RING
                    if is_bn(k) and (i >= STATS_RING or not first):
                        wait_apart(sp, bn_done, n * bn_slots + (i // DVE_SHARE if i >= STATS_RING else 0))
                    elif not is_bn(k) and (i >= STATS_RING or not first):
                        wait_apart(sp, act_done, 2 * (n * act_slots + (act_index(i - STATS_RING) + 1 if i >= STATS_RING else 0)))
                    sp.dma_start(stats_in[:, k, :], at_batch(x, n, KEPT + i)).then_inc(stats_loaded[k], 16)
                else:
                    s = i - streamed
                    if not first:
                        wait_apart(sp, kept_stored[s], n * 16)
                    sp.dma_start(kept[:, s, :], at_batch(x, n, s)).then_inc(kept_loaded[s], 16)

            def period(b, own, before, nxt):
                for step in steps(own, before, nxt):
                    if (s := behind(step, LAG_STORE, own, before)) is not None:
                        done = kept_stored[s] if s < KEPT else stream_stored[(s - KEPT) % STREAM_RING]
                        wait_apart(sp, finished, b * slots + step - LAG_STORE + 1)
                        b_of = b if step >= LAG_STORE else b - 1
                        sp.dma_start(at_batch(out, b_of, s), place(s)).then_inc(done, 16)
                    s = step + LEAD
                    if own and KEPT <= s < slots:
                        k, turn = (s - KEPT) % STREAM_RING, (s - KEPT) // STREAM_RING
                        if before or turn:
                            wait_apart(sp, stream_stored[k], (b * rounds + turn) * 16)
                        sp.dma_start(stream[:, k, :], at_batch(x, b, s)).then_inc(stream_loaded[k], 16)
                    if nxt:
                        for ahead in range(LEAD + 1) if step == 0 else [LEAD]:
                            for i in stats_items(step + ahead):
                                load_stats(b + 1, i, not own)

            over_periods(sp, period)
            for k in range(KEPT):
                wait_apart(sp, kept_stored[k], batches * 16)
            for k in range(STREAM_RING):
                wait_apart(sp, stream_stored[k], batches * rounds * 16)

        @block.gpsimd
        def _(pool):
            def period(b, own, before, nxt):
                for step in steps(own, before, nxt):
                    new_set = own and step >= SPLIT or before and step < SPLIT
                    if new_set and step % SPLIT == 1:
                        wait_apart(pool, miss_scaled, b * sets + step // SPLIT)
                        nc.gpsimd.tensor_tensor(miss[:, :], miss[:, :], approx[:, :], ALU.mult).then_inc(miss_squared, 1)
                    if own:
                        if step == 0:
                            wait_apart(pool, gn_step, (b + 1) * GN_STEPS)
                            if before:
                                wait_apart(pool, normed, b * slots)
                            nc.gpsimd.tensor_copy(norm_scalars[:, :], new_scalars[:, 0:2]).then_inc(norm_scalars_set, 1)
                            wait_apart(pool, norm_scalars_set, b + 1)
                        if step >= KEPT:
                            k, turn = (step - KEPT) % STREAM_RING, (step - KEPT) // STREAM_RING
                            wait_apart(pool, stream_loaded[k], (b * rounds + turn + 1) * 16)
                        nc.gpsimd.tensor_scalar(place(step), place(step), norm_scalars[:, 0:1], norm_scalars[:, 1:2],
                                                ALU.add, ALU.mult).then_inc(normed, 1)
                    if new_set and step % SPLIT == 0:
                        wait_apart(pool, root_sq_done, b * sets + step // SPLIT)
                        nc.gpsimd.tensor_tensor(miss[:, :], var[:, :], miss[:, :], ALU.subtract).then_inc(miss_done, 1)
                    if (s := behind(step, LAG_OUT, own, before)) is not None:
                        if s == 0:
                            if before:
                                wait_apart(pool, finished, b * slots)
                            nc.gpsimd.tensor_copy(out_shift[:, :], mean).then_inc(out_shift_set, 1)
                            wait_apart(pool, out_shift_set, b + 1)
                        wait_apart(pool, gated, b * slots + step - LAG_OUT + 1)
                        nc.gpsimd.tensor_scalar(place(s), place(s), 1.0, out_shift[:, 0:1],
                                                ALU.mult, ALU.add).then_inc(finished, 1)

            over_periods(pool, period)

        @block.scalar
        def _(act):
            act.wait_ge(consts_loaded, 64)

            def stats(n, i):
                data = wait_stats_data(act, n, i)
                a = act_index(i)
                if i == 1:
                    act.wait_ge(bn_done, n * bn_slots + 1)
                for which, function in enumerate((ACT.Identity, ACT.Square)):
                    before = 2 * (n * act_slots + a) + which
                    if not isinstance(n, int) or before >= 2:
                        act.wait_ge(act_done, before - 1)
                    nc.scalar.activation(unused[:, which, :], data, function, bias=pivot, scale=-1.0,
                                         accum_out=act_sums[:, which, a:a + 1]).then_inc(act_done, 1)

            def period(b, own, before, nxt):
                for step in steps(own, before, nxt):
                    new_set = own and step >= SPLIT or before and step < SPLIT
                    ready = b * sets + step // SPLIT
                    if new_set and step % SPLIT == 0:
                        act.wait_ge(summed, b * slots + step)
                        nc.scalar.activation(sum_sq[:, :], sums_ps[:, 0, :], ACT.Square).then_inc(sum_sq_done, 1)
                    if new_set and step % SPLIT == 2:
                        act.wait_ge(rest_done, ready)
                        nc.scalar.copy(piece[:, :], factor[:, :]).then_inc(piece_b_done, 1)
                    if own:
                        act.wait_ge(normed, b * slots + step + 1)
                        if before or step >= 2:
                            act.wait_ge(summed, b * slots + step - 1)
                        nc.scalar.activation(squares[:, step % 2, :], place(step), ACT.Square).then_inc(squared, 1)
                    if new_set and step % SPLIT == 0:
                        act.wait_ge(var_done, ready)
                        nc.scalar.activation(root[:, :], var[:, :], ACT.Sqrt).then_inc(root_done, 1)
                        act.wait_ge(root_done, ready)
                        nc.scalar.activation(miss[:, :], root[:, :], ACT.Square).then_inc(root_sq_done, 1)
                    if new_set and step % SPLIT == 1:
                        act.wait_ge(factor_done, ready)
                        nc.scalar.copy(piece[:, :], factor[:, :]).then_inc(piece_a_done, 1)
                    if nxt:
                        for i in stats_items(step):
                            if not is_bn(i):
                                stats(b + 1, i)
                    if nxt and step == slots - 1:
                        act.wait_ge(gn_step, (b + 1) * GN_STEPS + 12)
                        nc.scalar.activation(gn[:, 9:10], gn[:, 8:9], ACT.Sqrt).then_inc(gn_root_done, 1)

            over_periods(act, period)

        @block.vector
        def _(dve):
            dve.wait_ge(consts_loaded, 64)
            nc.vector.reduce_sum(w_sum[:, :], w_in, AXIS_X).then_inc(w_sum_ready, 1)
            dve.wait_ge(w_sum_ready, 1)
            nc.vector.tensor_scalar(w_sum[:, :], w_sum[:, :], 1.0 / P, None, ALU.mult).then_inc(w_sum_ready, 1)
            dve.wait_ge(w_sum_ready, 2)
            nc.vector.tensor_scalar(w_centred, w_in, w_sum[:, 0:1], None, ALU.subtract).then_inc(w_centred_ready, 1)
            dve.wait_ge(w_turned, 1)
            nc.vector.tensor_copy(w_t[:, :], small_ps[:, 0:P]).then_inc(w_ready, 1)

            def gn_scalars(n):
                done = [0]

                def then(instruction):
                    done[0] += 1
                    instruction.then_inc(gn_step, 1)
                    dve.wait_ge(gn_step, n * GN_STEPS + done[0])

                def cell(i, m=1):
                    return gn[:, i:i + m]

                total = bn_pixels + act_pixels
                wait_apart(dve, bn_done, (n + 1) * bn_slots)
                then(nc.vector.bn_aggr(cell(0, 2), bn[:, :, :].rearrange("p a b -> p (a b)")))
                dve.wait_ge(act_done, (n + 1) * 2 * act_slots)
                then(nc.vector.reduce_sum(cell(2, 2), act_sums[:, :, :], AXIS_X))
                then(nc.vector.tensor_scalar(cell(2, 2), cell(2, 2), 1.0 / total, None, ALU.mult))
                then(nc.vector.tensor_scalar(cell(4), cell(0), pivot, None, ALU.subtract))
                then(nc.vector.scalar_tensor_tensor(out=cell(5), in0=cell(4), scalar=cell(4), in1=cell(1),
                                                    op0=ALU.mult, op1=ALU.add))
                then(nc.vector.scalar_tensor_tensor(out=cell(4), in0=cell(4), scalar=bn_pixels / total, in1=cell(2),
                                                    op0=ALU.mult, op1=ALU.subtract))
                then(nc.vector.scalar_tensor_tensor(out=cell(5), in0=cell(5), scalar=bn_pixels / total, in1=cell(3),
                                                    op0=ALU.mult, op1=ALU.add))
                then(nc.vector.scalar_tensor_tensor(out=cell(5), in0=cell(4), scalar=cell(4), in1=cell(5),
                                                    op0=ALU.mult, op1=ALU.subtract))
                then(nc.vector.tensor_scalar(cell(6), cell(4), pivot, None, ALU.add))
                dve.wait_ge(group_mean_done, n + 1)
                then(nc.vector.tensor_scalar(cell(7), cell(6), small_ps[:, 0:1], None, ALU.subtract))
                then(nc.vector.scalar_tensor_tensor(out=cell(7), in0=cell(7), scalar=cell(7), in1=cell(5),
                                                    op0=ALU.mult, op1=ALU.subtract))
                dve.wait_ge(group_var_done, n + 1)
                then(nc.vector.tensor_scalar(cell(8), small_ps[:, 1:2], 0.0, GN_EPS, ALU.max, ALU.add))
                dve.wait_ge(gn_root_done, n + 1)
                then(nc.vector.reciprocal(cell(10), cell(9)))
                then(nc.vector.scalar_tensor_tensor(out=cell(11), in0=cell(8), scalar=cell(10), in1=cell(9),
                                                    op0=ALU.mult, op1=ALU.add))
                then(nc.vector.tensor_scalar(cell(11), cell(11), 0.5, None, ALU.mult))
                if isinstance(n, bass.RuntimeValue) or n > 0:
                    dve.wait_ge(out_shift_set, n)
                then(nc.vector.tensor_scalar(neg_mean, small_ps[:, 0:1], -1.0, None, ALU.mult))
                then(nc.vector.tensor_copy(mean, small_ps[:, 0:1]))
                then(nc.vector.tensor_scalar(gate_new, cell(11), bias_sb[:, 0:1], None, ALU.add))
                then(nc.vector.reciprocal(inv_std, cell(11)))
                assert done[0] == GN_STEPS

            def period(b, own, before, nxt):
                for step in steps(own, before, nxt):
                    new_set = own and step >= SPLIT or before and step < SPLIT
                    ready = b * sets + step // SPLIT

                    def scale():
                        if (s := behind(step, LAG_FACTOR, own, before)) is None:
                            return
                        count = b * slots + step - LAG_FACTOR
                        dve.wait_ge(factors_spread, count + 1)
                        if before or s >= 2:
                            dve.wait_ge(projected, count - 1)
                        nc.vector.tensor_tensor(scaled[:, s % 2, :], place(s), factor_ps[:, :], ALU.mult)\
                            .then_inc(scaled_done, 1)

                    def gate():
                        if (s := behind(step, LAG_OUT, own, before)) is None:
                            return
                        if s == 0:
                            if before:
                                dve.wait_ge(gated, b * slots)
                            nc.vector.tensor_copy(gate_shift[:, :], gate_new).then_inc(gate_shift_set, 1)
                            dve.wait_ge(gate_shift_set, b + 1)
                        dve.wait_ge(projected, b * slots + step - LAG_OUT + 1)
                        nc.vector.scalar_tensor_tensor(out=place(s), in0=proj_ps[:, s % 2, :], scalar=gate_shift[:, 0:1],
                                                       in1=place(s), op0=ALU.add, op1=ALU.mult).then_inc(gated, 1)

                    if new_set and step % SPLIT == 0:
                        dve.wait_ge(sum_sq_done, ready)
                        nc.vector.scalar_tensor_tensor(out=var[:, :], in0=sum_sq[:, :], scalar=-1.0 / P,
                                                       in1=sums_ps[:, 1, :], op0=ALU.mult, op1=ALU.add)\
                            .then_inc(var_sum_done, 1)
                        dve.wait_ge(var_sum_done, ready)
                        nc.vector.tensor_scalar(var[:, :], var[:, :], TINY, 1.0 / (P - 1), ALU.max, ALU.mult)\
                            .then_inc(var_done, 1)
                        scale()
                        dve.wait_ge(root_done, ready)
                        nc.vector.tensor_scalar(approx[:, :], root[:, :], NORM_EPS, None, ALU.add).then_inc(root_eps_done, 1)
                        gate()
                        dve.wait_ge(root_eps_done, ready)
                        nc.vector.reciprocal(approx[:, :], approx[:, :]).then_inc(approx_done, 1)
                    elif new_set and step % SPLIT == 1:
                        dve.wait_ge(approx_done, ready)
                        dve.wait_ge(miss_done, ready)
                        nc.vector.scalar_tensor_tensor(out=miss[:, :], in0=miss[:, :], scalar=-0.5, in1=approx[:, :],
                                                       op0=ALU.mult, op1=ALU.mult).then_inc(miss_scaled, 1)
                        scale()
                        dve.wait_ge(miss_squared, ready)
                        nc.vector.scalar_tensor_tensor(out=factor[:, :], in0=miss[:, :], scalar=1.0, in1=approx[:, :],
                                                       op0=ALU.add, op1=ALU.mult).then_inc(factor_done, 1)
                        gate()
                        dve.wait_ge(factor_done, ready)
                        dve.wait_ge(piece_a_done, ready)
                        nc.vector.scalar_tensor_tensor(out=factor[:, :], in0=piece[:, :], scalar=at["minus_bc"],
                                                       in1=factor[:, :], op0=ALU.mult, op1=ALU.add).then_inc(rest_done, 1)
                    elif new_set and step % SPLIT == 2:
                        gate()
                        dve.wait_ge(rest_done, ready)
                        dve.wait_ge(piece_b_done, ready)
                        nc.vector.scalar_tensor_tensor(out=pieces[:, :], in0=piece[:, :], scalar=at["minus_c"],
                                                       in1=factor[:, :], op0=ALU.mult, op1=ALU.add).then_inc(pieces_done, 1)
                        scale()
                    else:
                        scale()
                        gate()
                    if nxt:
                        for i in stats_items(step):
                            if is_bn(i):
                                data = wait_stats_data(dve, b + 1, i)
                                j = 2 * (i // DVE_SHARE)
                                nc.vector.bn_stats(bn[:, j, :], data[:, 0:BANK])
                                nc.vector.bn_stats(bn[:, j + 1, :], data[:, BANK:SLOT]).then_inc(bn_done, 1)
                    if nxt and step == slots - 1:
                        gn_scalars(b + 1)

            over_periods(dve, period)

        @block.tensor
        def _(pe):
            pe.wait_ge(consts_loaded, 64)
            pe.wait_ge(w_centred_ready, 1)
            nc.tensor.matmul(small_ps[:, 0:P], w_centred, at["ident"], start=True, stop=True).then_inc(w_turned, 1)
            pe.wait_ge(w_ready, 1)

            def spread(b, step, s):
                if s % SPLIT == 0:
                    pe.wait_ge(pieces_done, b * sets + (step - LAG_FACTOR) // SPLIT + 1)
                if step != LAG_FACTOR or not isinstance(b, int) or b > 0:
                    pe.wait_ge(scaled_done, b * slots + step - LAG_FACTOR)
                for t in range(TILES):
                    j = s % SPLIT * TILES + t
                    mm = nc.tensor.matmul(factor_ps[:, t * CHUNK:(t + 1) * CHUNK], pick_sb[:, j:j + 1].to_broadcast([P, P]), pieces[:, :],
                                          start=True, stop=True)
                mm.then_inc(factors_spread, 1)

            def sums(b, s, before):
                pe.wait_ge(squared, b * slots + s + 1)
                if s % SPLIT == 0 and (before or s):
                    pe.wait_ge(var_sum_done, b * sets + s // SPLIT)
                k = s % SPLIT
                rows = at["sum_rows"][:, 32 * k:32 * k + 32]
                for which, data in enumerate((place(s), squares[:, s % 2, :])):
                    for t in range(TILES):
                        mm = nc.tensor.matmul(sums_ps[32 * t:32 * t + 32, which, :], rows,
                                              data[:, t * CHUNK:(t + 1) * CHUNK],
                                              start=(which == 0 and k == 0), stop=(which == 1 and k == SPLIT - 1),
                                              skip_group_check=True)
                mm.then_inc(summed, 1)

            def project(b, step, s):
                count = b * slots + step - LAG_FACTOR
                pe.wait_ge(scaled_done, count + 1)
                if step >= LAG_FACTOR + 2 or not isinstance(b, int) or b > 0:
                    pe.wait_ge(gated, count - 1)
                for h in range(0, SLOT, BANK):
                    mm = nc.tensor.matmul(proj_ps[:, s % 2, h:h + BANK], w_t[:, :], scaled[:, s % 2, h:h + BANK],
                                          start=True, stop=True)
                mm.then_inc(projected, 1)

            def period(b, own, before, nxt):
                for step in steps(own, before, nxt):
                    s = behind(step, LAG_FACTOR, own, before)
                    if s is not None:
                        spread(b, step, s)
                    if own:
                        sums(b, step, before)
                    if s is not None:
                        project(b, step, s)
                if nxt:
                    pe.wait_ge(gn_step, (b + 1) * GN_STEPS + 9)
                    nc.tensor.matmul(small_ps[:, 0:1], at["group_avg"], gn[:, 6:7], start=True, stop=True)\
                        .then_inc(group_mean_done, 1)
                    pe.wait_ge(gn_step, (b + 1) * GN_STEPS + 11)
                    nc.tensor.matmul(small_ps[:, 1:2], at["group_avg"], gn[:, 7:8], start=True, stop=True)\
                        .then_inc(group_var_done, 1)

            over_periods(pe, period)


def kernel(x, L0_conv_W, L0_conv_b):
    import concourse.bacc as bacc
    from concourse.bass_utils import run_bass_kernel_spmd

    batches, channels, height, width = x.shape
    const, pick = constants(channels)
    arrays = {
        "x": np.ascontiguousarray(x).reshape(batches, channels, height * width),
        "w": np.ascontiguousarray(L0_conv_W),
        "bias": np.ascontiguousarray(L0_conv_b).reshape(channels, 1),
        "const": const,
        "pick": pick,
    }
    nc = bacc.Bacc("TRN2", target_bir_lowering=False, num_devices=1)
    args = [nc.dram_tensor(k, a.shape, mybir.dt.from_np(a.dtype), kind="ExternalInput").ap() for k, a in arrays.items()]
    out = nc.dram_tensor("out", arrays["x"].shape, F32, kind="ExternalOutput").ap()
    norm_gate_kernel(nc, *args, out)
    result = run_bass_kernel_spmd(nc, [arrays], core_ids=[0])
    return result.results[0]["out"].reshape(x.shape)
```

```python
import numpy as np

import concourse.bass as bass
from concourse import mybir
from contextlib import ExitStack

F32 = mybir.dt.float32
BF16 = mybir.dt.bfloat16
ALU = mybir.AluOpType
ACT = mybir.ActivationFunctionType
AXIS_X = mybir.AxisListType.X

P = 128
GROUPS = 32
GN_EPS = 1e-5
NORM_EPS = 1e-6
TINY = 1e-30

SLOT = 1024
CHUNK = 256
TILES = 4
SPLIT = 4
BANK = 512
COPIES = 32 // SPLIT

KEPT = 26
STREAM_RING = 14
STATS_RING = 4
DVE_SHARE = 4

LAG_VAR, LAG_ROOT, LAG_FIT, LAG_PIECES = 4, 5, 6, 7
LAG_SPREAD = 7
LAG_FACTOR = 8
LAG_OUT = 9
LAG_STORE = 10
NORM_LEAD = 1
LEAD = 3
STATS_LEAD = 2

CONST_COLS = {"ident": P, "group_avg": P, "sum_rows": SPLIT * 32, "minus_bc": 1, "minus_c": 1}


def constants(channels):
    per = channels // GROUPS
    row = np.arange(P)
    piece = row % 32 // SPLIT
    parts = {
        "ident": np.eye(P),
        "group_avg": (row[:, None] // per == row[None] // per) / per,
        "sum_rows": np.tile(np.arange(32)[None] % SPLIT == np.arange(SPLIT)[:, None], (P, 1, 1)).reshape(P, -1),
        "minus_bc": -((piece == 1) | (piece == 2)).astype(np.float32)[:, None],
        "minus_c": -(piece == 2).astype(np.float32)[:, None],
    }
    const = np.concatenate([parts[k].astype(np.float32) for k in CONST_COLS], axis=1)
    pick = np.zeros((P, SPLIT, TILES), np.float32)
    for k in range(SPLIT):
        for t in range(TILES):
            pick[(row // 32 == t) & (row % SPLIT == k) & (piece < 3), k, t] = 1.0
    return const, pick.reshape(P, -1).astype(mybir.dt.np(BF16))


def norm_gate_kernel(nc, x, w, bias, const, pick, out):
    batches, _, pixels = x.shape
    slots = pixels // SLOT
    sets = slots // SPLIT
    streamed = slots - KEPT
    uses = [len(range(k, streamed, STREAM_RING)) for k in range(STREAM_RING)]
    stats_uses = [len(range(k, streamed, STATS_RING)) for k in range(STATS_RING)]
    bn_slots = slots // DVE_SHARE
    act_slots = slots - bn_slots
    bn_pixels, act_pixels = bn_slots * SLOT, act_slots * SLOT
    assert slots * SLOT == pixels

    early = 28
    early_items = early * 3 // 2
    late_steps = slots - early - 5
    stats_step = [i * 2 // 3 if i < early_items else early + (i - early_items) * late_steps // (slots - early_items)
                  for i in range(slots)]

    def stats_items(step):
        return [i for i in range(slots) if stats_step[i] == step]

    with ExitStack() as ctx:
        def sb(name, shape, dt=F32):
            return ctx.enter_context(nc.sbuf_tensor(name, shape, dt))

        def ps(name, shape):
            return ctx.enter_context(nc.psum_tensor(name, shape, F32))

        def sem(name):
            return ctx.enter_context(nc.semaphore(name))

        kept = sb("kept", [P, KEPT, SLOT])
        stream = sb("stream", [P, STREAM_RING, SLOT])
        stats_in = sb("stats_in", [P, STATS_RING, SLOT])
        squares = sb("squares", [P, 2, SLOT])
        scaled = sb("scaled", [P, 2, SLOT])
        unused = sb("unused", [P, 2, SLOT], BF16)
        const_sb = sb("const_sb", [P, sum(CONST_COLS.values())])
        pick_sb = sb("pick_sb", [P, SPLIT * TILES], BF16)
        w_t = sb("w_t", [P, P])
        bias_sb = sb("bias_sb", [P, 1])
        w_sum = sb("w_sum", [P, 1])
        bn = sb("bn", [P, 2 * bn_slots, 6])
        act_sums = sb("act_sums", [P, 2, act_slots])
        gn = sb("gn", [P, 16])
        new_scalars = sb("new_scalars", [P, 4])
        norm_scalars = sb("norm_scalars", [P, 2])
        gate_shift = sb("gate_shift", [P, 1])
        out_shift = sb("out_shift", [P, 1])
        sum_sq = sb("sum_sq", [P, CHUNK])
        var = sb("var", [P, CHUNK])
        root = sb("root", [P, CHUNK])
        approx = sb("approx", [P, CHUNK])
        miss = sb("miss", [P, CHUNK])
        piece = sb("piece", [P, CHUNK], BF16)
        pieces = sb("pieces", [P, 2, CHUNK], BF16)

        factor = sum_sq

        sums_ps = ps("sums_ps", [P, 2, 2, CHUNK])
        small_ps = sums_ps[:, 0, 0, :]
        factor_ps = ps("factor_ps", [P, SLOT])
        proj_ps = ps("proj_ps", [P, 2, SLOT])

        at, col = {}, 0
        for name, n in CONST_COLS.items():
            at[name] = const_sb[:, col:col + n]
            col += n
        w_in = scaled[:, 0, 0:P]
        w_centred = scaled[:, 0, P:2 * P]
        pivot = bn[:, 0, 1:2]
        neg_mean, inv_std, mean, gate_new = (new_scalars[:, i:i + 1] for i in range(4))

        consts_loaded = sem("consts_loaded")
        kept_loaded = [sem(f"kept_loaded{i}") for i in range(KEPT)]
        kept_stored = [sem(f"kept_stored{i}") for i in range(KEPT)]
        stream_loaded = [sem(f"stream_loaded{i}") for i in range(STREAM_RING)]
        stream_stored = [sem(f"stream_stored{i}") for i in range(STREAM_RING)]
        stats_loaded = [sem(f"stats_loaded{i}") for i in range(STATS_RING)]
        w_sum_ready = sem("w_sum_ready")
        w_centred_ready = sem("w_centred_ready")
        w_turned = sem("w_turned")
        w_ready = sem("w_ready")
        bn_done = sem("bn_done")
        act_done = sem("act_done")
        gn_step = sem("gn_step")
        group_mean_done = sem("group_mean_done")
        group_var_done = sem("group_var_done")
        gn_root_done = sem("gn_root_done")
        norm_scalars_set = sem("norm_scalars_set")
        gate_shift_set = sem("gate_shift_set")
        out_shift_set = sem("out_shift_set")
        normed = sem("normed")
        squared = sem("squared")
        summed = sem("summed")
        factors_spread = sem("factors_spread")
        scaled_done = sem("scaled_done")
        projected = sem("projected")
        gated = sem("gated")
        finished = sem("finished")
        sum_sq_done = sem("sum_sq_done")
        var_sum_done = sem("var_sum_done")
        var_done = sem("var_done")
        root_done = sem("root_done")
        root_sq_done = sem("root_sq_done")
        root_eps_done = sem("root_eps_done")
        approx_done = sem("approx_done")
        miss_done = sem("miss_done")
        miss_scaled = sem("miss_scaled")
        miss_squared = sem("miss_squared")
        factor_done = sem("factor_done")
        piece_a_done = sem("piece_a_done")
        rest_done = sem("rest_done")
        piece_b_done = sem("piece_b_done")
        pieces_done = sem("pieces_done")
        wait_passed = sem("wait_passed")
        GN_STEPS = 19
        GN_STEP = slots - 4

        def wait_apart(eng, semaphore, value):
            eng.wait_ge(semaphore, value)
            if not isinstance(value, int):
                eng.sem_inc(wait_passed, 1)

        def place(s):
            return kept[:, s, :] if s < KEPT else stream[:, (s - KEPT) % STREAM_RING, :]

        def steps(own, before, nxt):
            return range(slots if own or nxt else LAG_STORE)

        def behind(step, lag, own, before, nxt=False):
            s = step - lag
            return s % slots if (before if s < 0 else own if s < slots else nxt) else None

        def set_behind(step, lag, b, own, before):
            if (step - lag) % SPLIT or behind(step, lag, own, before) is None:
                return None
            return b * sets + (step - lag) // SPLIT + 1

        def sums_of(s):
            return sums_ps[:, s // SPLIT % 2, :, :]

        def is_bn(i):
            return i % DVE_SHARE == 0

        def act_index(i):
            return i - i // DVE_SHARE - 1

        def wait_stats_data(eng, n, i):
            if i < streamed:
                k = i % STATS_RING
                eng.wait_ge(stats_loaded[k], (n * stats_uses[k] + i // STATS_RING + 1) * 16)
                return stats_in[:, k, :]
            eng.wait_ge(kept_loaded[i - streamed], (n + 1) * 16)
            return kept[:, i - streamed, :]

        def over_periods(eng, period):
            period(-1, own=False, before=False, nxt=True)
            period(0, own=True, before=False, nxt=batches > 1)
            if batches > 2:
                with eng.Fori(1, batches - 1) as b:
                    period(b, own=True, before=True, nxt=True)
            if batches > 1:
                period(batches - 1, own=True, before=True, nxt=False)
            period(batches, own=False, before=True, nxt=False)

        block = ctx.enter_context(nc.Block())

        @block.sync
        def _(sp):
            sp.dma_start(const_sb[:, :], const).then_inc(consts_loaded, 16)
            sp.dma_start(pick_sb[:, :], pick).then_inc(consts_loaded, 16)
            sp.dma_start(w_in, w).then_inc(consts_loaded, 16)
            sp.dma_start(bias_sb[:, :], bias).then_inc(consts_loaded, 16)

            def columns(s):
                return slice(s * SLOT, (s + 1) * SLOT)

            def at_batch(array, b, s):
                if isinstance(b, int):
                    return array[b, :, columns(s)]
                return array[bass.ds(b, 1), :, columns(s)].rearrange("a c n -> (a c) n")

            def load_stats(n, i, first):
                if i < streamed:
                    k = i % STATS_RING
                    last = i - STATS_RING
                    if last >= 0 and is_bn(last):
                        wait_apart(sp, bn_done, n * bn_slots + last // DVE_SHARE + 1)
                    elif last >= 0:
                        wait_apart(sp, act_done, 2 * (n * act_slots + act_index(last) + 1))
                    elif not first:
                        wait_apart(sp, bn_done, n * bn_slots)
                        wait_apart(sp, act_done, 2 * n * act_slots)
                    sp.dma_start(stats_in[:, k, :], at_batch(x, n, KEPT + i)).then_inc(stats_loaded[k], 16)
                else:
                    s = i - streamed
                    if not first:
                        wait_apart(sp, kept_stored[s], n * 16)
                    sp.dma_start(kept[:, s, :], at_batch(x, n, s)).then_inc(kept_loaded[s], 16)

            def period(b, own, before, nxt):
                for step in steps(own, before, nxt):
                    if (s := behind(step, LAG_STORE, own, before)) is not None:
                        done = kept_stored[s] if s < KEPT else stream_stored[(s - KEPT) % STREAM_RING]
                        wait_apart(sp, finished, b * slots + step - LAG_STORE + 1)
                        b_of = b if step >= LAG_STORE else b - 1
                        sp.dma_start(at_batch(out, b_of, s), place(s)).then_inc(done, 16)
                    s = step + LEAD
                    if own and KEPT <= s < slots:
                        k, turn = (s - KEPT) % STREAM_RING, (s - KEPT) // STREAM_RING
                        if before or turn:
                            wait_apart(sp, stream_stored[k], (b * uses[k] + turn) * 16)
                        sp.dma_start(stream[:, k, :], at_batch(x, b, s)).then_inc(stream_loaded[k], 16)
                    if nxt:
                        for ahead in range(STATS_LEAD + 1) if step == 0 else [STATS_LEAD]:
                            for i in stats_items(step + ahead):
                                load_stats(b + 1, i, not own)

            over_periods(sp, period)
            for k in range(KEPT):
                wait_apart(sp, kept_stored[k], batches * 16)
            for k in range(STREAM_RING):
                wait_apart(sp, stream_stored[k], batches * uses[k] * 16)

        @block.gpsimd
        def _(pool):
            def period(b, own, before, nxt):
                for step in steps(own, before, nxt):
                    if (fit := set_behind(step, LAG_FIT, b, own, before)) is not None:
                        wait_apart(pool, miss_scaled, fit)
                        nc.gpsimd.tensor_tensor(miss[:, :], miss[:, :], approx[:, :], ALU.mult).then_inc(miss_squared, 1)
                    if (s := behind(step, -NORM_LEAD, own, before, nxt)) is not None:
                        batch = b if step + NORM_LEAD < slots else b + 1
                        if s == 0:
                            wait_apart(pool, gn_step, (batch + 1) * GN_STEPS)
                            if own:
                                wait_apart(pool, normed, batch * slots)
                            nc.gpsimd.tensor_copy(norm_scalars[:, :], new_scalars[:, 0:2]).then_inc(norm_scalars_set, 1)
                            wait_apart(pool, norm_scalars_set, batch + 1)
                        if s >= KEPT:
                            k, turn = (s - KEPT) % STREAM_RING, (s - KEPT) // STREAM_RING
                            wait_apart(pool, stream_loaded[k], (batch * uses[k] + turn + 1) * 16)
                        nc.gpsimd.tensor_scalar(place(s), place(s), norm_scalars[:, 0:1], norm_scalars[:, 1:2],
                                                ALU.add, ALU.mult).then_inc(normed, 1)
                    if (of_root := set_behind(step, LAG_ROOT, b, own, before)) is not None:
                        wait_apart(pool, root_sq_done, of_root)
                        nc.gpsimd.tensor_tensor(miss[:, :], var[:, :], miss[:, :], ALU.subtract).then_inc(miss_done, 1)
                    if (s := behind(step, LAG_OUT, own, before)) is not None:
                        if s == 0:
                            if before:
                                wait_apart(pool, finished, b * slots)
                            nc.gpsimd.tensor_copy(out_shift[:, :], mean).then_inc(out_shift_set, 1)
                            wait_apart(pool, out_shift_set, b + 1)
                        wait_apart(pool, gated, b * slots + step - LAG_OUT + 1)
                        nc.gpsimd.tensor_scalar(place(s), place(s), 1.0, out_shift[:, 0:1],
                                                ALU.mult, ALU.add).then_inc(finished, 1)

            over_periods(pool, period)

        @block.scalar
        def _(act):
            act.wait_ge(consts_loaded, 64)

            def stats(n, i):
                data = wait_stats_data(act, n, i)
                a = act_index(i)
                if i == 1:
                    act.wait_ge(bn_done, n * bn_slots + 1)
                for which, function in enumerate((ACT.Identity, ACT.Square)):
                    before = 2 * (n * act_slots + a) + which
                    if not isinstance(n, int) or before >= 2:
                        act.wait_ge(act_done, before - 1)
                    nc.scalar.activation(unused[:, which, :], data, function, bias=pivot, scale=-1.0,
                                         accum_out=act_sums[:, which, a:a + 1]).then_inc(act_done, 1)

            def period(b, own, before, nxt):
                for step in steps(own, before, nxt):
                    if (done := set_behind(step, LAG_ROOT, b, own, before)) is not None:
                        act.wait_ge(var_done, done)
                        nc.scalar.activation(root[:, :], var[:, :], ACT.Sqrt).then_inc(root_done, 1)
                    if (pieces_of := set_behind(step, LAG_PIECES, b, own, before)) is not None:
                        act.wait_ge(rest_done, pieces_of)
                        nc.scalar.copy(piece[:, :], factor[:, :]).then_inc(piece_b_done, 1)
                    if own:
                        act.wait_ge(normed, b * slots + step + 1)
                        if before or step >= 2:
                            act.wait_ge(summed, b * slots + step - 1)
                        nc.scalar.activation(squares[:, step % 2, :], place(step), ACT.Square).then_inc(squared, 1)
                    if done is not None:
                        act.wait_ge(root_done, done)
                        nc.scalar.activation(miss[:, :], root[:, :], ACT.Square).then_inc(root_sq_done, 1)
                    if (fit := set_behind(step, LAG_FIT, b, own, before)) is not None:
                        act.wait_ge(factor_done, fit)
                        nc.scalar.copy(piece[:, :], factor[:, :]).then_inc(piece_a_done, 1)
                    if (of_var := set_behind(step, LAG_VAR, b, own, before)) is not None:
                        act.wait_ge(summed, b * slots + step)
                        nc.scalar.activation(sum_sq[:, :], sums_of(step - LAG_VAR)[:, 0, :], ACT.Square).then_inc(sum_sq_done, 1)
                    if nxt:
                        for i in stats_items(step):
                            if not is_bn(i):
                                stats(b + 1, i)
                    if nxt and step == GN_STEP + 2:
                        act.wait_ge(gn_step, (b + 1) * GN_STEPS + 12)
                        nc.scalar.activation(gn[:, 9:10], gn[:, 8:9], ACT.Sqrt).then_inc(gn_root_done, 1)

            over_periods(act, period)

        @block.vector
        def _(dve):
            dve.wait_ge(consts_loaded, 64)
            nc.vector.reduce_sum(w_sum[:, :], w_in, AXIS_X).then_inc(w_sum_ready, 1)
            dve.wait_ge(w_sum_ready, 1)
            nc.vector.tensor_scalar(w_sum[:, :], w_sum[:, :], 1.0 / P, None, ALU.mult).then_inc(w_sum_ready, 1)
            dve.wait_ge(w_sum_ready, 2)
            nc.vector.tensor_scalar(w_centred, w_in, w_sum[:, 0:1], None, ALU.subtract).then_inc(w_centred_ready, 1)
            dve.wait_ge(w_turned, 1)
            nc.vector.tensor_copy(w_t[:, :], small_ps[:, 0:P]).then_inc(w_ready, 1)

            def gn_scalars(n, part):
                done = [(0, 9, 11, 12)[part]]

                def then(instruction):
                    done[0] += 1
                    instruction.then_inc(gn_step, 1)
                    dve.wait_ge(gn_step, n * GN_STEPS + done[0])

                def cell(i, m=1):
                    return gn[:, i:i + m]

                if part == 0:
                    total = bn_pixels + act_pixels
                    wait_apart(dve, bn_done, (n + 1) * bn_slots)
                    then(nc.vector.bn_aggr(cell(0, 2), bn[:, :, :].rearrange("p a b -> p (a b)")))
                    dve.wait_ge(act_done, (n + 1) * 2 * act_slots)
                    then(nc.vector.reduce_sum(cell(2, 2), act_sums[:, :, :], AXIS_X))
                    then(nc.vector.tensor_scalar(cell(2, 2), cell(2, 2), 1.0 / total, None, ALU.mult))
                    then(nc.vector.tensor_scalar(cell(4), cell(0), pivot, None, ALU.subtract))
                    then(nc.vector.scalar_tensor_tensor(out=cell(5), in0=cell(4), scalar=cell(4), in1=cell(1),
                                                        op0=ALU.mult, op1=ALU.add))
                    then(nc.vector.scalar_tensor_tensor(out=cell(4), in0=cell(4), scalar=bn_pixels / total, in1=cell(2),
                                                        op0=ALU.mult, op1=ALU.subtract))
                    then(nc.vector.scalar_tensor_tensor(out=cell(5), in0=cell(5), scalar=bn_pixels / total, in1=cell(3),
                                                        op0=ALU.mult, op1=ALU.add))
                    then(nc.vector.scalar_tensor_tensor(out=cell(5), in0=cell(4), scalar=cell(4), in1=cell(5),
                                                        op0=ALU.mult, op1=ALU.subtract))
                    then(nc.vector.tensor_scalar(cell(6), cell(4), pivot, None, ALU.add))
                elif part == 1:
                    dve.wait_ge(group_mean_done, n + 1)
                    then(nc.vector.tensor_scalar(cell(7), cell(6), small_ps[:, 0:1], None, ALU.subtract))
                    then(nc.vector.scalar_tensor_tensor(out=cell(7), in0=cell(7), scalar=cell(7), in1=cell(5),
                                                        op0=ALU.mult, op1=ALU.subtract))
                elif part == 2:
                    dve.wait_ge(group_var_done, n + 1)
                    then(nc.vector.tensor_scalar(cell(8), small_ps[:, 1:2], 0.0, GN_EPS, ALU.max, ALU.add))
                else:
                    dve.wait_ge(gn_root_done, n + 1)
                    then(nc.vector.reciprocal(cell(10), cell(9)))
                    then(nc.vector.scalar_tensor_tensor(out=cell(11), in0=cell(8), scalar=cell(10), in1=cell(9),
                                                        op0=ALU.mult, op1=ALU.add))
                    then(nc.vector.tensor_scalar(cell(11), cell(11), 0.5, None, ALU.mult))
                    if not isinstance(n, int) or n > 0:
                        dve.wait_ge(out_shift_set, n)
                    then(nc.vector.tensor_scalar(neg_mean, small_ps[:, 0:1], -1.0, None, ALU.mult))
                    then(nc.vector.tensor_copy(mean, small_ps[:, 0:1]))
                    then(nc.vector.tensor_scalar(gate_new, cell(11), bias_sb[:, 0:1], None, ALU.add))
                    then(nc.vector.reciprocal(inv_std, cell(11)))
                    assert done[0] == GN_STEPS

            def period(b, own, before, nxt):
                for step in steps(own, before, nxt):
                    def scale():
                        if (s := behind(step, LAG_FACTOR, own, before)) is None:
                            return
                        count = b * slots + step - LAG_FACTOR
                        dve.wait_ge(factors_spread, count + 1)
                        if before or s >= 2:
                            dve.wait_ge(projected, count - 1)
                        nc.vector.tensor_tensor(scaled[:, s % 2, :], place(s), factor_ps[:, :], ALU.mult)\
                            .then_inc(scaled_done, 1)

                    def gate():
                        if (s := behind(step, LAG_OUT, own, before)) is None:
                            return
                        if s == 0:
                            if before:
                                dve.wait_ge(gated, b * slots)
                            nc.vector.tensor_copy(gate_shift[:, :], gate_new).then_inc(gate_shift_set, 1)
                            dve.wait_ge(gate_shift_set, b + 1)
                        dve.wait_ge(projected, b * slots + step - LAG_OUT + 1)
                        nc.vector.scalar_tensor_tensor(out=place(s), in0=proj_ps[:, s % 2, :], scalar=gate_shift[:, 0:1],
                                                       in1=place(s), op0=ALU.add, op1=ALU.mult).then_inc(gated, 1)

                    if (ready := set_behind(step, LAG_PIECES, b, own, before)) is not None:
                        dve.wait_ge(rest_done, ready)
                        dve.wait_ge(piece_b_done, ready)
                        nc.vector.scalar_tensor_tensor(out=pieces[:, (step - LAG_PIECES) // SPLIT % 2, :], in0=piece[:, :], scalar=at["minus_c"],
                                                       in1=factor[:, :], op0=ALU.mult, op1=ALU.add).then_inc(pieces_done, 1)
                    scale()
                    if (ready := set_behind(step, LAG_ROOT, b, own, before)) is not None:
                        dve.wait_ge(root_done, ready)
                        nc.vector.tensor_scalar(approx[:, :], root[:, :], NORM_EPS, None, ALU.add).then_inc(root_eps_done, 1)
                        dve.wait_ge(root_eps_done, ready)
                        nc.vector.reciprocal(approx[:, :], approx[:, :]).then_inc(approx_done, 1)
                    if (ready := set_behind(step, LAG_FIT, b, own, before)) is not None:
                        dve.wait_ge(miss_squared, ready)
                        nc.vector.scalar_tensor_tensor(out=factor[:, :], in0=miss[:, :], scalar=1.0, in1=approx[:, :],
                                                       op0=ALU.add, op1=ALU.mult).then_inc(factor_done, 1)
                    gate()
                    if (ready := set_behind(step, LAG_VAR, b, own, before)) is not None:
                        dve.wait_ge(sum_sq_done, ready)
                        nc.vector.scalar_tensor_tensor(out=var[:, :], in0=sum_sq[:, :], scalar=-1.0 / P,
                                                       in1=sums_of(step - LAG_VAR)[:, 1, :], op0=ALU.mult, op1=ALU.add)\
                            .then_inc(var_sum_done, 1)
                        dve.wait_ge(var_sum_done, ready)
                        nc.vector.tensor_scalar(var[:, :], var[:, :], TINY, 1.0 / (P - 1), ALU.max, ALU.mult)\
                            .then_inc(var_done, 1)
                    if (ready := set_behind(step, LAG_ROOT, b, own, before)) is not None:
                        dve.wait_ge(approx_done, ready)
                        dve.wait_ge(miss_done, ready)
                        nc.vector.scalar_tensor_tensor(out=miss[:, :], in0=miss[:, :], scalar=-0.5, in1=approx[:, :],
                                                       op0=ALU.mult, op1=ALU.mult).then_inc(miss_scaled, 1)
                    if (ready := set_behind(step, LAG_FIT, b, own, before)) is not None:
                        dve.wait_ge(factor_done, ready)
                        dve.wait_ge(piece_a_done, ready)
                        nc.vector.scalar_tensor_tensor(out=factor[:, :], in0=piece[:, :], scalar=at["minus_bc"],
                                                       in1=factor[:, :], op0=ALU.mult, op1=ALU.add).then_inc(rest_done, 1)
                    if nxt:
                        for i in stats_items(step):
                            if is_bn(i):
                                data = wait_stats_data(dve, b + 1, i)
                                j = 2 * (i // DVE_SHARE)
                                nc.vector.bn_stats(bn[:, j, :], data[:, 0:BANK])
                                nc.vector.bn_stats(bn[:, j + 1, :], data[:, BANK:SLOT]).then_inc(bn_done, 1)
                    if nxt and GN_STEP <= step <= GN_STEP + 2:
                        gn_scalars(b + 1, step - GN_STEP)
                    if nxt and step == GN_STEP + 2:
                        gn_scalars(b + 1, 3)

            over_periods(dve, period)

        @block.tensor
        def _(pe):
            pe.wait_ge(consts_loaded, 64)
            pe.wait_ge(w_centred_ready, 1)
            nc.tensor.matmul(small_ps[:, 0:P], w_centred, at["ident"], start=True, stop=True).then_inc(w_turned, 1)
            pe.wait_ge(w_ready, 1)

            def spread(b, step, s):
                if s % SPLIT == 0:
                    pe.wait_ge(pieces_done, b * sets + (step - LAG_SPREAD) // SPLIT + 1)
                if step != LAG_SPREAD or not isinstance(b, int) or b > 0:
                    pe.wait_ge(scaled_done, b * slots + step - LAG_SPREAD)
                for t in range(TILES):
                    j = s % SPLIT * TILES + t
                    mm = nc.tensor.matmul(factor_ps[:, t * CHUNK:(t + 1) * CHUNK], pick_sb[:, j:j + 1].to_broadcast([P, P]),
                                          pieces[:, s // SPLIT % 2, :],
                                          start=True, stop=True)
                mm.then_inc(factors_spread, 1)

            def sums(b, s, before):
                pe.wait_ge(squared, b * slots + s + 1)
                if s % SPLIT == 0 and (before or s >= 2 * SPLIT):
                    pe.wait_ge(var_sum_done, b * sets + s // SPLIT - 1)
                k = s % SPLIT
                rows = at["sum_rows"][:, 32 * k:32 * k + 32]
                for which, data in enumerate((place(s), squares[:, s % 2, :])):
                    for t in range(TILES):
                        mm = nc.tensor.matmul(sums_of(s)[32 * t:32 * t + 32, which, :], rows,
                                              data[:, t * CHUNK:(t + 1) * CHUNK],
                                              start=(which == 0 and k == 0), stop=(which == 1 and k == SPLIT - 1),
                                              skip_group_check=True)
                mm.then_inc(summed, 1)

            def project(b, step, s):
                count = b * slots + step - LAG_FACTOR
                pe.wait_ge(scaled_done, count + 1)
                if step >= LAG_FACTOR + 2 or not isinstance(b, int) or b > 0:
                    pe.wait_ge(gated, count - 1)
                for h in range(0, SLOT, BANK):
                    mm = nc.tensor.matmul(proj_ps[:, s % 2, h:h + BANK], w_t[:, :], scaled[:, s % 2, h:h + BANK],
                                          start=True, stop=True)
                mm.then_inc(projected, 1)

            def period(b, own, before, nxt):
                for step in steps(own, before, nxt):
                    if (s := behind(step, LAG_SPREAD, own, before)) is not None:
                        spread(b, step, s)
                    if (s := behind(step, LAG_FACTOR, own, before)) is not None:
                        project(b, step, s)
                    if own:
                        sums(b, step, before)
                    if nxt and step == GN_STEP:
                        pe.wait_ge(gn_step, (b + 1) * GN_STEPS + 9)
                        nc.tensor.matmul(small_ps[:, 0:1], at["group_avg"], gn[:, 6:7], start=True, stop=True)\
                            .then_inc(group_mean_done, 1)
                    if nxt and step == GN_STEP + 1:
                        pe.wait_ge(gn_step, (b + 1) * GN_STEPS + 11)
                        nc.tensor.matmul(small_ps[:, 1:2], at["group_avg"], gn[:, 7:8], start=True, stop=True)\
                            .then_inc(group_var_done, 1)

            over_periods(pe, period)


def kernel(x, L0_conv_W, L0_conv_b):
    import concourse.bacc as bacc
    from concourse.bass_utils import run_bass_kernel_spmd

    batches, channels, height, width = x.shape
    const, pick = constants(channels)
    arrays = {
        "x": np.ascontiguousarray(x).reshape(batches, channels, height * width),
        "w": np.ascontiguousarray(L0_conv_W),
        "bias": np.ascontiguousarray(L0_conv_b).reshape(channels, 1),
        "const": const,
        "pick": pick,
    }
    nc = bacc.Bacc("TRN2", target_bir_lowering=False, num_devices=1)
    args = [nc.dram_tensor(k, a.shape, mybir.dt.from_np(a.dtype), kind="ExternalInput").ap() for k, a in arrays.items()]
    out = nc.dram_tensor("out", arrays["x"].shape, F32, kind="ExternalOutput").ap()
    norm_gate_kernel(nc, *args, out)
    result = run_bass_kernel_spmd(nc, [arrays], core_ids=[0])
    return result.results[0]["out"].reshape(x.shape)
```

```python
import numpy as np

import concourse.bass as bass
from concourse import mybir
from contextlib import ExitStack

F32 = mybir.dt.float32
BF16 = mybir.dt.bfloat16
ALU = mybir.AluOpType
ACT = mybir.ActivationFunctionType
AXIS_X = mybir.AxisListType.X

P = 128
GROUPS = 32
GN_EPS = 1e-5
NORM_EPS = 1e-6
TINY = 1e-30

SLOT = 1024
CHUNK = 256
TILES = 4
SPLIT = 4
BANK = 512
COPIES = 32 // SPLIT

KEPT = 31
KEPT_FIRST = 8
KEPT_UNTIL = 46
SHARED_RING = 4
STREAM_RING = 14
EARLY_DROPS = 22
EARLY_RING = 8

STATS_ALL = [4, 4, 6, 5, 4, 5, 5, 6, 5, 4, 4, 3, 3, 4, 2]
STATS_DVE = [1, 2, 2, 2, 2, 2, 2, 2, 2, 2, 2, 0, 0, 1, 0]
DVE_PHASES = (3, 2, 0, 1)
PIVOT_STEP = 0
FIRST_ALL = [6, 6, 4] * 4
FIRST_DVE = [4, 3, 3] * 4

LAG_VAR, LAG_ROOT, LAG_FIT = 4, 5, 6
LAG_SPREAD = 7
LAG_FACTOR = 8
LAG_OUT = 9
LAG_STORE = 10
NORM_LEAD = 1
LEAD = 3
PREFETCHED = 3
FIRST_LOADS = 4
STATS_LEAD = 2

CONST_COLS = {"group_avg": P, "sum_rows": SPLIT * 32, "rows_bc": 1, "rows_c": 1, "norm_eps": 1}


def constants(channels):
    per = channels // GROUPS
    row = np.arange(P)
    piece = row % 32 // SPLIT
    parts = {
        "group_avg": (row[:, None] // per == row[None] // per) / per,
        "sum_rows": np.tile(np.arange(32)[None] % SPLIT == np.arange(SPLIT)[:, None], (P, 1, 1)).reshape(P, -1),
        "rows_bc": ((piece == 1) | (piece == 2)).astype(np.float32)[:, None],
        "rows_c": (piece == 2).astype(np.float32)[:, None],
        "norm_eps": np.full((P, 1), NORM_EPS),
    }
    const = np.concatenate([parts[k].astype(np.float32) for k in CONST_COLS], axis=1)
    pick = np.zeros((P, SPLIT, TILES), np.float32)
    for k in range(SPLIT):
        for t in range(TILES):
            pick[(row // 32 == t) & (row % SPLIT == k) & (piece < 3), k, t] = -0.5
    return const, pick.reshape(P, -1).astype(mybir.dt.np(BF16)), np.eye(P, dtype=np.float32)


def plan_statistics(takes, takes_dve):
    begun = []
    for k, (count, dve) in enumerate(zip(takes, takes_dve)):
        passes = 2 * (count - dve)
        steps = [max(k * SPLIT + p * SPLIT // passes, PIVOT_STEP + 1) for p in range(passes)]
        for p in range(0, passes, 2):
            begun.append((steps[p] + 0.5, "act", steps[p:p + 2]))
        for d in range(dve):
            step = k * SPLIT + (PIVOT_STEP if k == 0 and d == 0 else DVE_PHASES[d])
            begun.append((step, "dve", [step]))
    begun.sort()
    return Plan(begun)


class Plan:
    def __init__(self, begun):
        self.engine = [engine for _, engine, _ in begun]
        self.begin = [steps[0] for _, _, steps in begun]
        self.steps = [steps for _, _, steps in begun]
        self.index = [self.engine[:i].count(e) for i, e in enumerate(self.engine)]
        self.bn_slots, self.act_slots = self.engine.count("dve"), self.engine.count("act")

    def at(self, step, engine):
        return [(i, p) for i, steps in enumerate(self.steps) if self.engine[i] == engine
                for p, t in enumerate(steps) if t == step]


def norm_gate_kernel(nc, x, w, bias, const, pick, ident, out):
    batches, _, pixels = x.shape
    slots = pixels // SLOT
    sets = slots // SPLIT
    others = KEPT - KEPT_FIRST
    kept_slots = list(range(KEPT_FIRST)) + [KEPT_FIRST + i * (KEPT_UNTIL - KEPT_FIRST) // others for i in range(others)]
    streamed_slots = [s for s in range(slots) if s not in kept_slots]
    streamed = len(streamed_slots)
    assert list(range(SHARED_RING)) == kept_slots[:SHARED_RING]

    def drop_place(i):
        if i < EARLY_DROPS:
            return "stream", (streamed - STREAM_RING + i % EARLY_RING) % STREAM_RING
        return "shared", (i - EARLY_DROPS) % SHARED_RING

    def drops_in(place):
        return [i for i in range(streamed) if drop_place(i) == place]

    stream_uses = [len(range(k, streamed, STREAM_RING)) for k in range(STREAM_RING)]
    assert slots * SLOT == pixels

    plan = plan_statistics(STATS_ALL, STATS_DVE)
    first_plan = plan_statistics(FIRST_ALL, FIRST_DVE)
    assert len(plan.begin) == len(first_plan.begin) == slots

    def bn_before(n):
        return 0 if isinstance(n, int) and n == 0 else n * plan.bn_slots + (first_plan.bn_slots - plan.bn_slots)

    def act_before(n):
        if isinstance(n, int) and n == 0:
            return 0
        return n * (2 * plan.act_slots) + 2 * (first_plan.act_slots - plan.act_slots)

    with ExitStack() as ctx:
        def sb(name, shape, dt=F32):
            return ctx.enter_context(nc.sbuf_tensor(name, shape, dt))

        def ps(name, shape):
            return ctx.enter_context(nc.psum_tensor(name, shape, F32))

        def sem(name):
            return ctx.enter_context(nc.semaphore(name))

        kept = sb("kept", [P, KEPT - SHARED_RING, SLOT])
        stream = sb("stream", [P, STREAM_RING, SLOT])
        shared = sb("shared", [P, SHARED_RING, SLOT])
        squares = sb("squares", [P, 2, SLOT])
        scaled = sb("scaled", [P, 2, SLOT])
        unused = sb("unused", [P, 2, SLOT], mybir.dt.uint8)
        const_sb = sb("const_sb", [P, sum(CONST_COLS.values())])
        pick_sb = sb("pick_sb", [P, SPLIT * TILES], BF16)
        w_t = sb("w_t", [P, P])
        bias_sb = sb("bias_sb", [P, 1])
        w_sum = sb("w_sum", [P, 1])
        bn = sb("bn", [P, 2 * plan.bn_slots, 6])
        act_sums = sb("act_sums", [P, 2, max(plan.act_slots, first_plan.act_slots)])
        gn = sb("gn", [P, 16])
        new_scalars = sb("new_scalars", [P, 4])
        norm_scalars = sb("norm_scalars", [P, 2])
        gate_shift = sb("gate_shift", [P, 1])
        out_shift = sb("out_shift", [P, 1])
        sum_sq = sb("sum_sq", [P, CHUNK])
        var = sb("var", [P, CHUNK])
        root = sb("root", [P, CHUNK])
        approx = sb("approx", [P, CHUNK])
        miss = sb("miss", [P, CHUNK])
        piece = sb("piece", [P, CHUNK], BF16)
        pieces = sb("pieces", [P, 2, CHUNK], BF16)

        factor = sum_sq

        sums_ps = ps("sums_ps", [P, 2, 2, CHUNK])
        small_ps = sums_ps[:, 0, 0, :]
        factor_ps = ps("factor_ps", [P, SLOT])
        proj_ps = ps("proj_ps", [P, 2, SLOT])

        at, col = {}, 0
        for name, n in CONST_COLS.items():
            at[name] = const_sb[:, col:col + n]
            col += n
        w_in = scaled[:, 0, 0:P]
        w_centred = scaled[:, 0, P:2 * P]
        ident_sb = scaled[:, 0, 2 * P:3 * P]
        bn_first = scaled[:, 1, 0:2 * first_plan.bn_slots * 6].rearrange("p (a b) -> p a b", b=6)
        neg_mean, inv_std, mean, gate_new = (new_scalars[:, i:i + 1] for i in range(4))

        consts_loaded = sem("consts_loaded")
        kept_loaded = [sem(f"kept_loaded{i}") for i in range(KEPT)]
        kept_stored = [sem(f"kept_stored{i}") for i in range(KEPT)]
        stream_loaded = [sem(f"stream_loaded{i}") for i in range(STREAM_RING)]
        stream_stored = [sem(f"stream_stored{i}") for i in range(STREAM_RING)]
        drop_loaded = {("stream", k): sem(f"stream_drop_loaded{k}") for k in range(STREAM_RING) if drops_in(("stream", k))}
        drop_loaded |= {("shared", k): sem(f"shared_drop_loaded{k}") for k in range(SHARED_RING)}
        w_sum_ready = sem("w_sum_ready")
        w_centred_ready = sem("w_centred_ready")
        w_turned = sem("w_turned")
        w_ready = sem("w_ready")
        bn_done = sem("bn_done")
        act_done = sem("act_done")
        gn_step = sem("gn_step")
        group_mean_done = sem("group_mean_done")
        group_var_done = sem("group_var_done")
        gn_root_done = sem("gn_root_done")
        norm_scalars_set = sem("norm_scalars_set")
        gate_shift_set = sem("gate_shift_set")
        out_shift_set = sem("out_shift_set")
        normed = sem("normed")
        squared = sem("squared")
        summed = sem("summed")
        factors_spread = sem("factors_spread")
        scaled_done = sem("scaled_done")
        projected = sem("projected")
        gated = sem("gated")
        finished = sem("finished")
        sum_sq_done = sem("sum_sq_done")
        var_sum_done = sem("var_sum_done")
        var_done = sem("var_done")
        root_done = sem("root_done")
        root_sq_done = sem("root_sq_done")
        root_eps_done = sem("root_eps_done")
        approx_done = sem("approx_done")
        miss_done = sem("miss_done")
        miss_scaled = sem("miss_scaled")
        miss_squared = sem("miss_squared")
        factor_done = sem("factor_done")
        piece_a_done = sem("piece_a_done")
        rest_done = sem("rest_done")
        piece_b_done = sem("piece_b_done")
        pieces_done = sem("pieces_done")
        SUM_SQ_AFTER = 1
        wait_passed = sem("wait_passed")
        GN_STEPS = 19
        GN_STEP = slots - 5

        def wait_apart(eng, semaphore, value):
            eng.wait_ge(semaphore, value)
            if not isinstance(value, int):
                eng.sem_inc(wait_passed, 1)

        def place(s):
            if s < SHARED_RING:
                return shared[:, s, :]
            if s in kept_slots:
                return kept[:, kept_slots.index(s) - SHARED_RING, :]
            return stream[:, streamed_slots.index(s) % STREAM_RING, :]

        def steps(own, before, nxt):
            return range(slots if own or nxt else LAG_STORE)

        def behind(step, lag, own, before, nxt=False):
            s = step - lag
            return s % slots if (before if s < 0 else own if s < slots else nxt) else None

        def set_behind(step, lag, b, own, before):
            if (step - lag) % SPLIT or behind(step, lag, own, before) is None:
                return None
            return b * sets + (step - lag) // SPLIT + 1

        def sums_of(s):
            return sums_ps[:, s // SPLIT % 2, :, :]

        def wait_stats_data(eng, n, i):
            if i < streamed:
                lies = drop_place(i)
                uses = drops_in(lies)
                eng.wait_ge(drop_loaded[lies], (n * len(uses) + uses.index(i) + 1) * 16)
                return {"stream": stream, "shared": shared}[lies[0]][:, lies[1], :]
            eng.wait_ge(kept_loaded[i - streamed], (n + 1) * 16)
            return place(kept_slots[i - streamed])

        def bn_of(of):
            return bn_first if of is first_plan else bn

        def pivot_of(of):
            return bn_of(of)[:, 0, 1:2]

        def over_periods(eng, period, looks_ahead=False):
            looped = batches - 1 - looks_ahead
            ahead = {"more": True} if looks_ahead else {}
            no_more = {"more": False} if looks_ahead else {}
            period(-1, own=False, before=False, nxt=True, **(ahead if batches > 1 else no_more))
            period(0, own=True, before=False, nxt=batches > 1, **(ahead if batches > 2 else no_more))
            if looped > 1:
                with eng.Fori(1, looped) as b:
                    period(b, own=True, before=True, nxt=True, **ahead)
            for b in range(max(looped, 1), batches):
                period(b, own=True, before=True, nxt=b < batches - 1, **no_more)
            period(batches, own=False, before=True, nxt=False, **no_more)

        block = ctx.enter_context(nc.Block())

        @block.sync
        def _(sp):
            sp.dma_start(const_sb[:, :], const).then_inc(consts_loaded, 16)
            sp.dma_start(pick_sb[:, :], pick).then_inc(consts_loaded, 16)
            sp.dma_start(w_in, w).then_inc(consts_loaded, 16)
            sp.dma_start(ident_sb, ident).then_inc(consts_loaded, 16)
            sp.dma_start(bias_sb[:, :], bias).then_inc(consts_loaded, 16)

            def columns(s):
                return slice(s * SLOT, (s + 1) * SLOT)

            def at_batch(array, b, s):
                if isinstance(b, int):
                    return array[b, :, columns(s)]
                return array[bass.ds(b, 1), :, columns(s)].rearrange("a c n -> (a c) n")

            def wait_item_done(n, i, of):
                if of.engine[i] == "dve":
                    wait_apart(sp, bn_done, bn_before(n) + (of.index[i] + 1))
                else:
                    wait_apart(sp, act_done, act_before(n) + 2 * (of.index[i] + 1))

            def load_stats(n, i, of, first, before):
                if i < streamed:
                    lies = drop_place(i)
                    kind, k = lies
                    turn = drops_in(lies).index(i)
                    if turn:
                        wait_item_done(n, drops_in(lies)[turn - 1], of)
                    else:
                        if not first:
                            wait_apart(sp, bn_done, bn_before(n))
                            wait_apart(sp, act_done, act_before(n))
                        if kind == "stream" and before:
                            wait_apart(sp, stream_stored[k], (n - 1) * (stream_uses[k] * 16))
                        if kind == "shared" and not first:
                            wait_apart(sp, kept_stored[k], n * 16)
                    to = stream if kind == "stream" else shared
                    sp.dma_start(to[:, k, :], at_batch(x, n, streamed_slots[i])).then_inc(drop_loaded[lies], 16)
                else:
                    k = i - streamed
                    if k < SHARED_RING:
                        wait_item_done(n, drops_in(("shared", k))[-1], of)
                    elif not first:
                        wait_apart(sp, kept_stored[k], n * 16)
                    s = kept_slots[k]
                    sp.dma_start(place(s), at_batch(x, n, s)).then_inc(kept_loaded[k], 16)

            def period(b, own, before, nxt, more):
                of = plan if own else first_plan
                for step in steps(own, before, nxt):
                    loaded = PREFETCHED if own else 0
                    if nxt and step == 0:
                        for i in range(loaded, FIRST_LOADS):
                            load_stats(b + 1, i, of, first=not own, before=before)
                    if (s := behind(step, LAG_STORE, own, before)) is not None:
                        if s in kept_slots:
                            done = kept_stored[kept_slots.index(s)]
                        else:
                            done = stream_stored[streamed_slots.index(s) % STREAM_RING]
                        wait_apart(sp, finished, b * slots + step - LAG_STORE + 1)
                        b_of = b if step >= LAG_STORE else b - 1
                        sp.dma_start(at_batch(out, b_of, s), place(s)).then_inc(done, 16)
                    s = step + LEAD
                    if own and s in streamed_slots:
                        turn, k = divmod(streamed_slots.index(s), STREAM_RING)
                        if nxt and not turn and drops_in(("stream", k)):
                            wait_item_done(b + 1, drops_in(("stream", k))[-1], of)
                        if before or turn:
                            wait_apart(sp, stream_stored[k], (b * stream_uses[k] + turn) * 16)
                        sp.dma_start(stream[:, k, :], at_batch(x, b, s)).then_inc(stream_loaded[k], 16)
                    if nxt:
                        for i, begin in enumerate(of.begin):
                            if i >= max(loaded, FIRST_LOADS) and (begin == step + STATS_LEAD or step == 0 and begin < STATS_LEAD):
                                load_stats(b + 1, i, of, first=not own, before=before)
                    if more and step >= slots - PREFETCHED:
                        load_stats(b + 2, step - (slots - PREFETCHED), plan, first=False, before=own)

            over_periods(sp, period, looks_ahead=True)
            for k in range(KEPT):
                wait_apart(sp, kept_stored[k], batches * 16)
            for k in range(STREAM_RING):
                wait_apart(sp, stream_stored[k], batches * stream_uses[k] * 16)

        @block.gpsimd
        def _(pool):
            def norm(b, step, s, own):
                batch = b if step + NORM_LEAD < slots else b + 1
                if s == 0:
                    wait_apart(pool, gn_step, (batch + 1) * GN_STEPS)
                    if own:
                        wait_apart(pool, normed, batch * slots)
                    nc.gpsimd.tensor_copy(norm_scalars[:, :], new_scalars[:, 0:2]).then_inc(norm_scalars_set, 1)
                    wait_apart(pool, norm_scalars_set, batch + 1)
                if s in streamed_slots:
                    turn, k = divmod(streamed_slots.index(s), STREAM_RING)
                    wait_apart(pool, stream_loaded[k], (batch * stream_uses[k] + turn + 1) * 16)
                nc.gpsimd.tensor_scalar(place(s), place(s), norm_scalars[:, 0:1], norm_scalars[:, 1:2],
                                        ALU.add, ALU.mult).then_inc(normed, 1)

            def finish(b, step, s, before):
                if s == 0:
                    if before:
                        wait_apart(pool, finished, b * slots)
                    nc.gpsimd.tensor_copy(out_shift[:, :], mean).then_inc(out_shift_set, 1)
                    wait_apart(pool, out_shift_set, b + 1)
                wait_apart(pool, gated, b * slots + step - LAG_OUT + 1)
                nc.gpsimd.tensor_scalar(place(s), place(s), 1.0, out_shift[:, 0:1],
                                        ALU.mult, ALU.add).then_inc(finished, 1)

            def correct(done):
                wait_apart(pool, approx_done, done)
                wait_apart(pool, miss_done, done)
                nc.gpsimd.tensor_tensor(miss[:, :], miss[:, :], approx[:, :], ALU.mult).then_inc(miss_scaled, 1)
                wait_apart(pool, miss_scaled, done)
                nc.gpsimd.tensor_tensor(miss[:, :], miss[:, :], approx[:, :], ALU.mult).then_inc(miss_squared, 1)

            def split_first(done):
                wait_apart(pool, piece_a_done, done)
                nc.gpsimd.tensor_tensor(factor[:, :], factor[:, :], piece[:, :], ALU.subtract).then_inc(rest_done, 1)

            def split_second(done, step):
                wait_apart(pool, piece_b_done, done)
                nc.gpsimd.tensor_tensor(pieces[:, (step - LAG_FIT) // SPLIT % 2, :], factor[:, :], piece[:, :],
                                        ALU.subtract).then_inc(pieces_done, 1)

            def period(b, own, before, nxt):
                for step in steps(own, before, nxt):
                    root_of = set_behind(step, LAG_ROOT, b, own, before)
                    fit_of = set_behind(step, LAG_FIT, b, own, before)
                    if (s := behind(step, -NORM_LEAD, own, before, nxt)) is not None:
                        norm(b, step, s, own)
                    if fit_of is not None:
                        split_first(fit_of)
                    if root_of is not None:
                        wait_apart(pool, root_sq_done, root_of)
                        nc.gpsimd.tensor_tensor(miss[:, :], var[:, :], miss[:, :], ALU.subtract).then_inc(miss_done, 1)
                        correct(root_of)
                    if (s := behind(step, LAG_OUT, own, before)) is not None:
                        finish(b, step, s, before)
                    if fit_of is not None:
                        split_second(fit_of, step)

            over_periods(pool, period)

        @block.scalar
        def _(act):
            act.wait_ge(consts_loaded, 80)

            def statistics(n, step, of, count):
                for i, which in todo[:count]:
                    data = wait_stats_data(act, n, i)
                    a = of.index[i]
                    if a == 0 and which == 0:
                        act.wait_ge(bn_done, bn_before(n) + 1)
                    done = 2 * a + which
                    if not isinstance(n, int) or n > 0 or done >= 2:
                        act.wait_ge(act_done, act_before(n) + (done - 1))
                    nc.scalar.activation(unused[:, which, :], data, (ACT.Identity, ACT.Square)[which], bias=pivot_of(of),
                                         scale=-1.0, accum_out=act_sums[:, which, a:a + 1]).then_inc(act_done, 1)
                del todo[:count]

            todo = []

            def period(b, own, before, nxt):
                of = plan if own else first_plan
                for step in steps(own, before, nxt):
                    if nxt:
                        todo.extend(of.at(step, "act"))
                    if own:
                        act.wait_ge(normed, b * slots + step + 1)
                        if before or step >= 2:
                            act.wait_ge(summed, b * slots + step - 1)
                        nc.scalar.activation(squares[:, step % 2, :], place(step), ACT.Square).then_inc(squared, 1)
                    if (done := set_behind(step, LAG_ROOT, b, own, before)) is not None:
                        act.wait_ge(var_done, done)
                        nc.scalar.activation(root[:, :], var[:, :], ACT.Sqrt).then_inc(root_done, 1)
                        act.wait_ge(root_done, done)
                        nc.scalar.add(approx[:, :], root[:, :], at["norm_eps"]).then_inc(root_eps_done, 1)
                        nc.scalar.activation(miss[:, :], root[:, :], ACT.Square).then_inc(root_sq_done, 1)
                    if (done := set_behind(step, LAG_FIT, b, own, before)) is not None:
                        act.wait_ge(factor_done, done)
                        nc.scalar.activation(piece[:, :], factor[:, :], ACT.Identity, scale=at["rows_bc"]).then_inc(piece_a_done, 1)
                        statistics(b + 1, step, of, 1)
                        act.wait_ge(rest_done, done)
                        nc.scalar.activation(piece[:, :], factor[:, :], ACT.Identity, scale=at["rows_c"]).then_inc(piece_b_done, 1)
                    if (done := set_behind(step, LAG_VAR, b, own, before)) is not None:
                        statistics(b + 1, step, of, SUM_SQ_AFTER)
                        act.wait_ge(summed, b * slots + step)
                        nc.scalar.activation(sum_sq[:, :], sums_of(step - LAG_VAR)[:, 0, :], ACT.Square).then_inc(sum_sq_done, 1)
                    statistics(b + 1, step, of, len(todo))
                    if nxt and step == GN_STEP + 3:
                        act.wait_ge(gn_step, (b + 1) * GN_STEPS + 12)
                        nc.scalar.activation(gn[:, 9:10], gn[:, 8:9], ACT.Sqrt).then_inc(gn_root_done, 1)

            over_periods(act, period)

        @block.vector
        def _(dve):
            dve.wait_ge(consts_loaded, 80)
            nc.vector.reduce_sum(w_sum[:, :], w_in, AXIS_X).then_inc(w_sum_ready, 1)
            dve.wait_ge(w_sum_ready, 1)
            nc.vector.tensor_scalar(w_sum[:, :], w_sum[:, :], 1.0 / P, None, ALU.mult).then_inc(w_sum_ready, 1)
            dve.wait_ge(w_sum_ready, 2)
            nc.vector.tensor_scalar(w_centred, w_in, w_sum[:, 0:1], None, ALU.subtract).then_inc(w_centred_ready, 1)
            dve.wait_ge(w_turned, 1)
            nc.vector.tensor_copy(w_t[:, :], small_ps[:, 0:P]).then_inc(w_ready, 1)

            def gn_scalars(n, part, of):
                done = [(0, 9, 11, 12)[part]]

                def then(instruction):
                    done[0] += 1
                    instruction.then_inc(gn_step, 1)
                    dve.wait_ge(gn_step, n * GN_STEPS + done[0])

                def cell(i, m=1):
                    return gn[:, i:i + m]

                if part == 0:
                    total = slots * SLOT
                    bn_part = of.bn_slots / slots
                    wait_apart(dve, bn_done, bn_before(n) + of.bn_slots)
                    then(nc.vector.bn_aggr(cell(0, 2), bn_of(of)[:, 0:2 * of.bn_slots, :].rearrange("p a b -> p (a b)")))
                    dve.wait_ge(act_done, act_before(n) + 2 * of.act_slots)
                    then(nc.vector.reduce_sum(cell(2, 2), act_sums[:, :, 0:of.act_slots], AXIS_X))
                    then(nc.vector.tensor_scalar(cell(2, 2), cell(2, 2), 1.0 / total, None, ALU.mult))
                    then(nc.vector.tensor_scalar(cell(4), cell(0), pivot_of(of), None, ALU.subtract))
                    then(nc.vector.scalar_tensor_tensor(out=cell(5), in0=cell(4), scalar=cell(4), in1=cell(1),
                                                        op0=ALU.mult, op1=ALU.add))
                    then(nc.vector.scalar_tensor_tensor(out=cell(4), in0=cell(4), scalar=bn_part, in1=cell(2),
                                                        op0=ALU.mult, op1=ALU.subtract))
                    then(nc.vector.scalar_tensor_tensor(out=cell(5), in0=cell(5), scalar=bn_part, in1=cell(3),
                                                        op0=ALU.mult, op1=ALU.add))
                    then(nc.vector.scalar_tensor_tensor(out=cell(5), in0=cell(4), scalar=cell(4), in1=cell(5),
                                                        op0=ALU.mult, op1=ALU.subtract))
                    then(nc.vector.tensor_scalar(cell(6), cell(4), pivot_of(of), None, ALU.add))
                elif part == 1:
                    dve.wait_ge(group_mean_done, n + 1)
                    then(nc.vector.tensor_scalar(cell(7), cell(6), small_ps[:, 0:1], None, ALU.subtract))
                    then(nc.vector.scalar_tensor_tensor(out=cell(7), in0=cell(7), scalar=cell(7), in1=cell(5),
                                                        op0=ALU.mult, op1=ALU.subtract))
                elif part == 2:
                    dve.wait_ge(group_var_done, n + 1)
                    then(nc.vector.tensor_scalar(cell(8), small_ps[:, 1:2], 0.0, GN_EPS, ALU.max, ALU.add))
                else:
                    dve.wait_ge(gn_root_done, n + 1)
                    then(nc.vector.reciprocal(cell(10), cell(9)))
                    then(nc.vector.scalar_tensor_tensor(out=cell(11), in0=cell(8), scalar=cell(10), in1=cell(9),
                                                        op0=ALU.mult, op1=ALU.add))
                    then(nc.vector.tensor_scalar(cell(11), cell(11), 0.5, None, ALU.mult))
                    if not isinstance(n, int) or n > 0:
                        dve.wait_ge(out_shift_set, n)
                    then(nc.vector.tensor_scalar(neg_mean, small_ps[:, 0:1], -1.0, None, ALU.mult))
                    then(nc.vector.tensor_copy(mean, small_ps[:, 0:1]))
                    then(nc.vector.tensor_scalar(gate_new, cell(11), bias_sb[:, 0:1], None, ALU.add))
                    then(nc.vector.reciprocal(inv_std, cell(11)))
                    assert done[0] == GN_STEPS

            def period(b, own, before, nxt):
                of = plan if own else first_plan
                for step in steps(own, before, nxt):
                    def scale():
                        if (s := behind(step, LAG_FACTOR, own, before)) is None:
                            return
                        count = b * slots + step - LAG_FACTOR
                        dve.wait_ge(factors_spread, count + 1)
                        if before or s >= 2:
                            dve.wait_ge(projected, count - 1)
                        nc.vector.tensor_tensor(scaled[:, s % 2, :], place(s), factor_ps[:, :], ALU.mult)\
                            .then_inc(scaled_done, 1)

                    def gate():
                        if (s := behind(step, LAG_OUT, own, before)) is None:
                            return
                        if s == 0:
                            if before:
                                dve.wait_ge(gated, b * slots)
                            nc.vector.tensor_copy(gate_shift[:, :], gate_new).then_inc(gate_shift_set, 1)
                            dve.wait_ge(gate_shift_set, b + 1)
                        dve.wait_ge(projected, b * slots + step - LAG_OUT + 1)
                        nc.vector.scalar_tensor_tensor(out=place(s), in0=proj_ps[:, s % 2, :], scalar=gate_shift[:, 0:1],
                                                       in1=place(s), op0=ALU.add, op1=ALU.mult).then_inc(gated, 1)

                    def var_of_sums(ready):
                        dve.wait_ge(sum_sq_done, ready)
                        nc.vector.scalar_tensor_tensor(out=var[:, :], in0=sum_sq[:, :], scalar=-1.0 / P,
                                                       in1=sums_of(step - LAG_VAR)[:, 1, :], op0=ALU.mult, op1=ALU.add)\
                            .then_inc(var_sum_done, 1)
                        dve.wait_ge(var_sum_done, ready)
                        nc.vector.tensor_scalar(var[:, :], var[:, :], TINY, 1.0 / (P - 1), ALU.max, ALU.mult)\
                            .then_inc(var_done, 1)

                    scale()
                    if nxt and step == GN_STEP + 3:
                        gn_scalars(b + 1, 2, of)
                    if (ready := set_behind(step, LAG_ROOT, b, own, before)) is not None:
                        dve.wait_ge(root_eps_done, ready)
                        nc.vector.reciprocal(approx[:, :], approx[:, :]).then_inc(approx_done, 1)
                    if (ready := set_behind(step, LAG_FIT, b, own, before)) is not None:
                        dve.wait_ge(miss_squared, ready)
                        nc.vector.scalar_tensor_tensor(out=factor[:, :], in0=miss[:, :], scalar=-2.0, in1=approx[:, :],
                                                       op0=ALU.add, op1=ALU.mult).then_inc(factor_done, 1)
                    gate()
                    if (ready := set_behind(step, LAG_VAR, b, own, before)) is not None:
                        var_of_sums(ready)
                    if nxt:
                        for i, _ in of.at(step, "dve"):
                            data = wait_stats_data(dve, b + 1, i)
                            j = 2 * of.index[i]
                            nc.vector.bn_stats(bn_of(of)[:, j, :], data[:, 0:BANK])
                            nc.vector.bn_stats(bn_of(of)[:, j + 1, :], data[:, BANK:SLOT]).then_inc(bn_done, 1)
                    if nxt and step == GN_STEP:
                        gn_scalars(b + 1, 0, of)
                    if nxt and step == GN_STEP + 2:
                        gn_scalars(b + 1, 1, of)
                    if nxt and step == GN_STEP + 3:
                        gn_scalars(b + 1, 3, of)

            over_periods(dve, period)

        @block.tensor
        def _(pe):
            pe.wait_ge(consts_loaded, 80)
            pe.wait_ge(w_centred_ready, 1)
            nc.tensor.matmul(small_ps[:, 0:P], w_centred, ident_sb, start=True, stop=True).then_inc(w_turned, 1)
            pe.wait_ge(w_ready, 1)

            def spread(b, step, s):
                if s % SPLIT == 0:
                    pe.wait_ge(pieces_done, b * sets + (step - LAG_SPREAD) // SPLIT + 1)
                if step != LAG_SPREAD or not isinstance(b, int) or b > 0:
                    pe.wait_ge(scaled_done, b * slots + step - LAG_SPREAD)
                for t in range(TILES):
                    j = s % SPLIT * TILES + t
                    mm = nc.tensor.matmul(factor_ps[:, t * CHUNK:(t + 1) * CHUNK], pick_sb[:, j:j + 1].to_broadcast([P, P]),
                                          pieces[:, s // SPLIT % 2, :],
                                          start=True, stop=True)
                mm.then_inc(factors_spread, 1)

            def sums(b, s, before):
                pe.wait_ge(squared, b * slots + s + 1)
                if s % SPLIT == 0 and (before or s >= 2 * SPLIT):
                    pe.wait_ge(var_sum_done, b * sets + s // SPLIT - 1)
                k = s % SPLIT
                rows = at["sum_rows"][:, 32 * k:32 * k + 32]
                for which, data in enumerate((place(s), squares[:, s % 2, :])):
                    for t in range(TILES):
                        mm = nc.tensor.matmul(sums_of(s)[32 * t:32 * t + 32, which, :], rows,
                                              data[:, t * CHUNK:(t + 1) * CHUNK],
                                              start=(which == 0 and k == 0), stop=(which == 1 and k == SPLIT - 1),
                                              skip_group_check=True)
                mm.then_inc(summed, 1)

            def project(b, step, s):
                count = b * slots + step - LAG_FACTOR
                pe.wait_ge(scaled_done, count + 1)
                if step >= LAG_FACTOR + 2 or not isinstance(b, int) or b > 0:
                    pe.wait_ge(gated, count - 1)
                for h in range(0, SLOT, BANK):
                    mm = nc.tensor.matmul(proj_ps[:, s % 2, h:h + BANK], w_t[:, :], scaled[:, s % 2, h:h + BANK],
                                          start=True, stop=True)
                mm.then_inc(projected, 1)

            def period(b, own, before, nxt):
                for step in steps(own, before, nxt):
                    if nxt and step == GN_STEP + 2:
                        pe.wait_ge(gn_step, (b + 1) * GN_STEPS + 9)
                        if own:
                            pe.wait_ge(var_sum_done, b * sets + (sets - 1))
                        nc.tensor.matmul(small_ps[:, 0:1], at["group_avg"], gn[:, 6:7], start=True, stop=True)\
                            .then_inc(group_mean_done, 1)
                    if nxt and step == GN_STEP + 3:
                        pe.wait_ge(gn_step, (b + 1) * GN_STEPS + 11)
                        nc.tensor.matmul(small_ps[:, 1:2], at["group_avg"], gn[:, 7:8], start=True, stop=True)\
                            .then_inc(group_var_done, 1)
                    if (s := behind(step, LAG_SPREAD, own, before)) is not None:
                        spread(b, step, s)
                    if (s := behind(step, LAG_FACTOR, own, before)) is not None:
                        project(b, step, s)
                    if own:
                        sums(b, step, before)

            over_periods(pe, period)


def kernel(x, L0_conv_W, L0_conv_b):
    import concourse.bacc as bacc
    from concourse.bass_utils import run_bass_kernel_spmd

    batches, channels, height, width = x.shape
    const, pick, ident = constants(channels)
    arrays = {
        "x": np.ascontiguousarray(x).reshape(batches, channels, height * width),
        "w": np.ascontiguousarray(L0_conv_W),
        "bias": np.ascontiguousarray(L0_conv_b).reshape(channels, 1),
        "const": const,
        "pick": pick,
        "ident": ident,
    }
    nc = bacc.Bacc("TRN2", target_bir_lowering=False, num_devices=1)
    args = [nc.dram_tensor(k, a.shape, mybir.dt.from_np(a.dtype), kind="ExternalInput").ap() for k, a in arrays.items()]
    out = nc.dram_tensor("out", arrays["x"].shape, F32, kind="ExternalOutput").ap()
    norm_gate_kernel(nc, *args, out)
    result = run_bass_kernel_spmd(nc, [arrays], core_ids=[0])
    return result.results[0]["out"].reshape(x.shape)
```
